# Optimizing a Trainium2 kernel written in Bass

```python
import numpy as np
import jax
import jax.numpy as jnp

def _softmax(x, axis=-1):
    return jax.nn.softmax(x, axis=axis)

def _gelu(x):
    return jax.nn.gelu(x, approximate=True)

def _silu(x):
    return jax.nn.silu(x)

def _sigmoid(x):
    return jax.nn.sigmoid(x)

def _layernorm(x, axis=-1, eps=1e-05):
    m = jnp.mean(x, axis=axis, keepdims=True)
    v = jnp.var(x, axis=axis, keepdims=True)
    return (x - m) / jnp.sqrt(v + eps)

def _scatter_add(tgt, idx, src, axis=0):
    return tgt.at[idx].add(src)

def _segment_sum(src, seg, n):
    return jax.ops.segment_sum(src, seg, n)
kernel_name = 'mk_recurrent_d1_jaxref_r8_71ec90'

def setup_inputs(seed: int=0):
    np.random.seed(seed)
    _w = jnp.asarray

    def _L0_attn_setup():
        import jax, jax.numpy as jnp
        import numpy as np
        DIM = 128
        DIM_INNER = 256
        B, S = (4, 512)

        def heinsen_associative_scan_log(log_coeffs, log_values):
            a_star = jnp.cumsum(log_coeffs, axis=1)
            log_h0_plus_b_star = jax.lax.cumlogsumexp(log_values - a_star, axis=1)
            return jnp.exp(a_star + log_h0_plus_b_star)
        key = jax.random.key(seed)
        k1, k2, k3 = jax.random.split(key, 3)
        x = jax.random.normal(k1, (B, S, DIM), dtype=jnp.float32)
        W_hg = jax.random.normal(k2, (DIM, 2 * DIM_INNER), dtype=jnp.float32) / np.sqrt(DIM)
        W_out = jax.random.normal(k3, (DIM_INNER, DIM), dtype=jnp.float32) / np.sqrt(DIM_INNER)
        return {'x': x, 'W_hg': W_hg, 'W_out': W_out}
    _L0_attn_in = _L0_attn_setup()

    def _L0_ffn_setup():
        import jax, jax.numpy as jnp
        import numpy as np
        B, S, D = (2, 256, 128)
        E, K, F = (16, 2, 64)
        FS = 128
        key = jax.random.key(seed)
        ks = jax.random.split(key, 8)

        def w(k, shape, fan_in):
            return jax.random.normal(k, shape, jnp.float32) / np.sqrt(fan_in).astype(np.float32)
        return {'x': jax.random.normal(ks[0], (B, S, D), jnp.float32), 'Wr': w(ks[1], (D, E), D), 'Wg': w(ks[2], (E, D, F), D), 'Wu': w(ks[3], (E, D, F), D), 'Wd': w(ks[4], (E, F, D), F), 'Sg': w(ks[5], (D, FS), D), 'Su': w(ks[6], (D, FS), D), 'Sd': w(ks[7], (FS, D), FS)}
    _L0_ffn_in = _L0_ffn_setup()
    _d = {'L0_attn_x': _L0_attn_in['x'], 'L0_attn_W_hg': _L0_attn_in['W_hg'], 'L0_attn_W_out': _L0_attn_in['W_out'], 'L0_ffn_Wr': _L0_ffn_in['Wr'], 'L0_ffn_Wg': _L0_ffn_in['Wg'], 'L0_ffn_Wu': _L0_ffn_in['Wu'], 'L0_ffn_Wd': _L0_ffn_in['Wd'], 'L0_ffn_Sg': _L0_ffn_in['Sg'], 'L0_ffn_Su': _L0_ffn_in['Su'], 'L0_ffn_Sd': _L0_ffn_in['Sd']}
    _x0 = _d['L0_attn_x']
    _d['L0_attn_x'] = jax.random.normal(jax.random.fold_in(jax.random.key(seed), 1), (32, 256, 128), dtype=_x0.dtype)
    del _x0
    return _d

def reference(L0_attn_x, L0_attn_W_hg, L0_attn_W_out, L0_ffn_Wr, L0_ffn_Wg, L0_ffn_Wu, L0_ffn_Wd, L0_ffn_Sg, L0_ffn_Su, L0_ffn_Sd):

    def _L0_attn_ref(x, W_hg, W_out):
        import jax, jax.numpy as jnp
        import numpy as np
        DIM = 128
        DIM_INNER = 256
        B, S = (4, 512)

        def heinsen_associative_scan_log(log_coeffs, log_values):
            a_star = jnp.cumsum(log_coeffs, axis=1)
            log_h0_plus_b_star = jax.lax.cumlogsumexp(log_values - a_star, axis=1)
            return jnp.exp(a_star + log_h0_plus_b_star)
        hg = jnp.einsum('bsd,de->bse', x, W_hg)
        hidden, gate = jnp.split(hg, 2, axis=-1)
        log_z = jax.nn.log_sigmoid(gate)
        log_coeffs = -jax.nn.softplus(gate)
        hidden_log = jnp.log(jax.nn.relu(hidden) + 0.5)
        log_values = hidden_log + log_z
        h = heinsen_associative_scan_log(log_coeffs, log_values)
        out = jnp.einsum('bse,ed->bsd', h, W_out)
        return out

    def _L0_ffn_ref(x, Wr, Wg, Wu, Wd, Sg, Su, Sd):
        import jax, jax.numpy as jnp
        import numpy as np
        B, S, D = (2, 256, 128)
        E, K, F = (16, 2, 64)
        FS = 128
        b, s, d = x.shape
        T = b * s
        xf = x.reshape(T, d)
        shared = jax.nn.silu(xf @ Sg) * (xf @ Su) @ Sd
        probs = jax.nn.softmax(xf @ Wr, axis=-1)
        topk_p, topk_i = jax.lax.top_k(probs, K)
        n_exp = Wr.shape[1]
        cw = jnp.zeros((T, n_exp), x.dtype).at[jnp.arange(T)[:, None], topk_i].add(topk_p)

        def step(acc, ew):
            wg, wu, wd, c = ew
            y = jax.nn.silu(xf @ wg) * (xf @ wu) @ wd
            return (acc + y * c[:, None], None)
        routed, _ = jax.lax.scan(step, jnp.zeros_like(xf), (Wg, Wu, Wd, cw.T))
        return (routed + shared).reshape(b, s, d)
    x = L0_attn_x
    xn = _layernorm(x, axis=-1)
    s = _L0_attn_ref(xn, L0_attn_W_hg, L0_attn_W_out)
    g = _silu(_L0_ffn_ref(xn, L0_ffn_Wr, L0_ffn_Wg, L0_ffn_Wu, L0_ffn_Wd, L0_ffn_Sg, L0_ffn_Su, L0_ffn_Sd))
    x = x + s * g
    return x

_drawn_inputs = setup_inputs


def setup_inputs(seed=0):
    import zlib

    import numpy as np

    out = dict(_drawn_inputs(seed))
    spreads = {}
    factors = {}
    for name, (base, spread) in spreads.items():
        noise = np.random.default_rng([zlib.crc32(name.encode()), seed]).standard_normal(out[name].shape)
        drawn = base * np.exp(spread * noise) if base else spread * noise
        out[name] = jnp.asarray(drawn.astype(out[name].dtype))
    for name, factor in factors.items():
        out[name] = (out[name] * factor).astype(out[name].dtype)
    return out
```

```python
from contextlib import ExitStack

import concourse.bass as bass
from concourse import mybir

F32 = mybir.dt.float32
F32R = mybir.dt.float32r
U32 = mybir.dt.uint32
ALU = mybir.AluOpType
ACT = mybir.ActivationFunctionType
AX = mybir.AxisListType

P = 128
CT = 512
TT = CT // P
NH = 2
NF = 9
SLOTS = NH + NF
LAG = 3


class Chunk:

    def __init__(self, i, par):
        self.i, self.par = i, par

    def at(self, d):
        return Chunk(self.i + (self.par + d) // 2, (self.par + d) % 2)

    def n(self, per, k=0):
        return self.i * (2 * per) + (self.par * per + k)

    def dma(self, times=1):
        return self.i * (16 * times) + 16 * times


def recurrent_moe_block(nc, x, W_hg, W_out, Wr, Wg, Wu, Wd, Sg, Su, Sd, out):
    B, S, D = x.shape
    E, _, F = Wg.shape
    T = B * S
    NCH = T // CT
    NB = E * F // P
    SEQS = CT // S
    assert D == P and NB + 1 == NF and NCH % 2 == 0 and NCH >= 4 and CT % S == 0

    x_tiles = x.rearrange("b s d -> (b s) d").rearrange("(c t p) d -> c p t d", p=P, t=TT)
    out_tiles = out.rearrange("b s d -> (b s) d").rearrange("(c t p) d -> c p t d", p=P, t=TT)
    cw_dram = nc.dram_tensor("cw_scratch", (2, E, CT), F32, kind="Internal").ap()

    with ExitStack() as ctx:
        def sb(name, shape, dt=F32):
            return ctx.enter_context(nc.sbuf_tensor(name, shape, dt))

        def sem(name):
            return ctx.enter_context(nc.semaphore(name))

        def sem2(name):
            return [sem(f"{name}{k}") for k in range(2)]

        WCOLS = [("r", E), ("hg", 4 * P), ("s", 2 * P), ("g", NB * P), ("u", NB * P),
                 ("o", NH * P), ("sd", P), ("d", NB * P)]
        off, at = {}, 0
        for name, cols in WCOLS:
            off[name] = at
            at += cols
        w_hi = sb("w_hi", [P, at], F32R)
        w_lo = sb("w_lo", [P, at], F32R)
        wr_both = sb("wr_both", [P, 2 * E], F32R)
        ident = sb("ident", [P, P])
        iota_e = sb("iota_e", [P, E])
        consts = sb("consts", [P, 3])
        eps = sb("eps", [P, TT])
        minus_half = sb("minus_half", [P, TT])

        x_in = sb("x_in", [P, 2, TT, P])
        x_out = sb("x_out", [P, 2, TT, P])
        xn = sb("xn", [P, TT, P])
        stats = sb("stats", [P, TT, 6])
        meanvar = sb("meanvar", [P, TT, 2])
        var_eps = sb("var_eps", [P, TT])
        rstd = sb("rstd", [P, TT])
        xT_hi = sb("xT_hi", [P, 2, CT], F32R)
        xT_lo = sb("xT_lo", [P, 2, CT], F32R)
        rec_z = sb("rec_z", [P, NH, CT])
        rec_a = sb("rec_a", [P, NH, CT])
        rec_v = sb("rec_v", [P, NH, CT])
        rec_h = sb("rec_h", [P, NH, CT])
        silu_g = sb("silu_g", [P, 2, CT])
        prod = sb("prod", [P, NF, CT])
        act_hi = sb("act_hi", [P, SLOTS, CT], F32R)
        act_lo = sb("act_lo", [P, SLOTS, CT], F32R)
        lgT = sb("lgT", [2 * E, CT])
        lg = sb("lg", [P, TT, E])
        top8 = sb("top8", [P, TT, 8])
        top8_at = sb("top8_at", [P, TT, 8], U32)
        shifted = sb("shifted", [P, TT, E])
        silu_n = sb("silu_n", [P, TT, E])
        silu_p = sb("silu_p", [P, TT, E])
        expv = sb("expv", [P, TT, E])
        esum = sb("esum", [P, TT])
        rsum = sb("rsum", [P, TT])
        mask0 = sb("mask0", [P, TT, E])
        mask1 = sb("mask1", [P, TT, E])
        cw_tok = sb("cw_tok", [P, E, TT])
        cwT = sb("cwT", [E * TT, P])
        cw = sb("cw", [P, 2, NB, CT])
        ffn_gate = sb("ffn_gate", [P, CT])
        sg = sb("sg", [P, CT])
        stage = prod[:, :, :].rearrange("p k n -> p (k n)")
        assert at <= NF * CT

        psum = lambda name: ctx.enter_context(nc.psum_tensor(name, [P, CT], F32))
        p_gate = [psum("p_gate0"), psum("p_gate1")]
        p_lin = [psum("p_lin0"), psum("p_lin1")]
        p_ffn = psum("p_ffn")
        p_rec = psum("p_rec")
        p_front = psum("p_front")
        p_out = psum("p_out")

        s_w = {name: sem(f"w_landed_{name}") for name, _ in WCOLS}
        s_hi_w, s_lo_w = sem("weights_hi"), sem("weights_lo")
        s_const0, s_const = sem("ident_zeroed"), sem("constants_ready")
        s_xin, s_xres, s_stored = sem2("x_landed"), sem2("residual_landed"), sem2("out_stored")
        s_cws, s_cwa, s_cwb = sem("cw_stored"), sem2("cw_first_half"), sem2("cw_second_half")
        s_stat, s_mv, s_ve, s_rstd, s_norm = (sem("bn_stats_done"), sem("mean_var_ready"), sem("var_eps_ready"),
                                              sem("rstd_ready"), sem("normalised"))
        s_xT, s_xhi, s_xlo = sem("xT_in_psum"), sem("xT_hi_ready"), sem("xT_lo_ready")
        s_rl, s_lgT, s_lt = sem("router_logits_T"), sem("logits_T_copied"), sem("router_logits")
        s_rt, s_shift, s_rsil, s_cwtok = sem("router_step"), sem("logits_shifted"), sem("router_silus"), sem("cw_ready")
        s_cwTp, s_cwT = sem("cwT_in_psum"), sem("cwT_copied")
        s_gate, s_lin = sem("gate_in_psum"), sem("linear_in_psum")
        s_tanh, s_relu, s_z, s_a, s_v, s_scan = (sem("tanh_done"), sem("relu_done"), sem("z_done"), sem("a_done"), sem("v_done"),
                                             sem("scan_done"))
        s_hhi, s_hlo = sem("rec_hi_ready"), sem("rec_lo_ready")
        s_silu, s_p, s_q = sem("silu_done"), sem("gated_done"), sem("weighted_done")
        s_fhi, s_flo, s_down = sem("ffn_hi_ready"), sem("ffn_lo_ready"), sem("down_done")
        s_rec, s_gsil, s_sg, s_ot, s_add = (sem("rec_out_done"), sem("ffn_gate_done"), sem("sg_done"),
                                            sem("out_in_psum"), sem("out_added"))
        block = ctx.enter_context(nc.Block())

        CONSTS = 7
        ROUTER_STEPS = 10

        def chunks(engine, chunk, end=None):
            chunk(Chunk(0, 0), 0)
            chunk(Chunk(0, 1), 1)
            with engine.Fori(1, NCH // 2 - 1) as i:
                chunk(Chunk(i, 0), None)
                chunk(Chunk(i, 1), None)
            chunk(Chunk(NCH // 2 - 1, 0), NCH - 2)
            chunk(Chunk(NCH // 2 - 1, 1), NCH - 1)

        def has(c, d):
            return c is None or 0 <= c + d < NCH

        def slot_par(ch, k):
            return (SLOTS * ch.par + k) % 2

        @block.sync
        def _(sp):
            def load_x(ch):
                if isinstance(ch.i, int) and ch.i == 0:
                    pass
                else:
                    sp.wait_ge(s_norm, ch.at(-2).n(1, 1))
                c = ch.i * 2 + ch.par
                sp.dma_start(x_in[:, ch.par], x_tiles[c]).then_inc(s_xin[ch.par], 16)

            load_x(Chunk(0, 0))
            load_x(Chunk(0, 1))

            def chunk(ch, c):
                if has(c, 2):
                    load_x(ch.at(2))
                if has(c, -2):
                    sp.wait_ge(s_stored[ch.par], ch.at(-2).dma())
                sp.dma_start(x_out[:, ch.par], x_tiles[ch.i * 2 + ch.par]).then_inc(s_xres[ch.par], 16)
                if has(c, -1):
                    store(ch.at(-1))
                if has(c, 1):
                    spread(ch.at(1), has(c, -1))

            def store(ch):
                sp.wait_ge(s_add, ch.n(1, 1))
                sp.dma_start(out_tiles[ch.i * 2 + ch.par], x_out[:, ch.par]).then_inc(s_stored[ch.par], 16)

            def spread(ch, reused):
                sp.wait_ge(s_cwT, ch.n(1, 1))
                if reused:
                    sp.wait_ge(s_cwb[ch.par], ch.at(-2).dma(2))
                sp.dma_start(cw_dram[ch.par].rearrange("e (t n) -> (e t) n", t=TT), cwT[:, :]).then_inc(s_cws, 16)
                sp.wait_ge(s_cws, ch.n(16, 16))
                if reused:
                    sp.wait_ge(s_q, ch.at(-2).n(NB, NB))
                for half, landed in ((0, s_cwa), (1, s_cwb)):
                    b0, b1 = half * NB // 2, (half + 1) * NB // 2
                    for e in range(2):
                        rows = cw_dram[ch.par, 2 * b0 + e:2 * b1:2, :]
                        spread_rows = bass.AP(tensor=rows.tensor, offset=rows.offset,
                                              ap=[[0, F]] + [list(d) for d in rows.ap])
                        sp.dma_start(cw[e * F:(e + 1) * F, ch.par, b0:b1, :], spread_rows)\
                          .then_inc(landed[ch.par], 16)

            spread(Chunk(0, 0), False)
            chunks(sp, chunk)
            last = Chunk(NCH // 2 - 1, 1)
            store(last)
            sp.wait_ge(s_stored[0], last.at(-1).dma())
            sp.wait_ge(s_stored[1], last.dma())
            sp.wait_ge(s_cws, last.n(16, 16))

        @block.gpsimd
        def _(pool):
            nc.gpsimd.memset(minus_half[:, :], -0.5).then_inc(s_const, 1)
            nc.gpsimd.memset(ident[:, :], 0.0).then_inc(s_const0, 1)
            pool.wait_ge(s_const0, 1)
            nc.gpsimd.affine_select(out=ident[:, :], in_=ident[:, :], compare_op=ALU.not_equal, fill=1.0, base=0,
                                    pattern=[[-1, P]], channel_multiplier=1).then_inc(s_const, 1)
            nc.gpsimd.iota(iota_e[:, :], [[1, E]], base=0, channel_multiplier=0,
                           allow_small_or_imprecise_dtypes=True).then_inc(s_const, 1)
            for col, value in enumerate((-1.0, 1.0, 0.5)):
                nc.gpsimd.memset(consts[:, col:col + 1], value).then_inc(s_const, 1)
            nc.gpsimd.memset(eps[:, :], 1e-5).then_inc(s_const, 1)
            pool.wait_ge(s_const, CONSTS)

            def rstd_of(ch):
                pool.wait_ge(s_mv, ch.n(1, 1))
                nc.gpsimd.tensor_tensor(var_eps[:, :], meanvar[:, :, 1], eps[:, :], ALU.add).then_inc(s_ve, 1)
                pool.wait_ge(s_ve, ch.n(1, 1))
                nc.gpsimd.tensor_tensor(rstd[:, :], var_eps[:, :], minus_half[:, :], ALU.pow).then_inc(s_rstd, 1)

            def decay(ch, j):
                pool.wait_ge(s_z, ch.n(NH, j + 1))
                nc.gpsimd.tensor_tensor(rec_a[:, j], consts[:, 1:2].to_broadcast([P, CT]), rec_z[:, j], ALU.subtract)\
                  .then_inc(s_a, 1)

            def rec_lo(ch, j):
                pool.wait_ge(s_hhi, ch.n(NH, j + 1))
                nc.gpsimd.tensor_tensor(act_lo[:, j], rec_h[:, j], act_hi[:, j].bitcast(F32), ALU.subtract)\
                  .then_inc(s_hlo, 1)

            def ffn_lo(ch, k):
                f = k - NH
                pool.wait_ge(s_fhi, ch.n(NF, f + 1))
                nc.gpsimd.tensor_tensor(act_lo[:, k], prod[:, f], act_hi[:, k].bitcast(F32), ALU.subtract)\
                  .then_inc(s_flo, 1)

            rstd_of(Chunk(0, 0))
            rstd_of(Chunk(0, 1))

            def chunk(ch, c):
                for k in range(SLOTS):
                    if k < NH:
                        decay(ch, k)
                    if k == 0 and has(c, -1):
                        ffn_lo(ch.at(-1), SLOTS - 1)
                    if k in (2, 3):
                        rec_lo(ch, k - 2)
                    if k == 9 and has(c, 2):
                        rstd_of(ch.at(2))
                    if k > NH:
                        ffn_lo(ch, k - 1)

            chunks(pool, chunk)
            ffn_lo(Chunk(NCH // 2 - 1, 1), SLOTS - 1)

        @block.scalar
        def _(act):
            def view(name, n):
                return stage[:, off[name]:off[name] + n]

            act.dma_start(view("r", E), Wr).then_inc(s_w["r"], 16)
            act.dma_start(view("hg", 4 * P), W_hg).then_inc(s_w["hg"], 16)
            act.dma_start(view("s", P), Sg).then_inc(s_w["s"], 16)
            act.dma_start(stage[:, off["s"] + P:off["s"] + 2 * P], Su).then_inc(s_w["s"], 16)
            act.dma_start(view("g", NB * P).rearrange("p (e f) -> p e f", f=F),
                          Wg.rearrange("e d f -> d e f")).then_inc(s_w["g"], 16)
            act.dma_start(view("u", NB * P).rearrange("p (e f) -> p e f", f=F),
                          Wu.rearrange("e d f -> d e f")).then_inc(s_w["u"], 16)
            act.dma_start(view("o", NH * P).rearrange("p (b d) -> p b d", d=P),
                          W_out.rearrange("(b p) d -> p b d", p=P)).then_inc(s_w["o"], 16)
            act.dma_start(view("sd", P), Sd).then_inc(s_w["sd"], 16)
            act.dma_start(view("d", NB * P).rearrange("p (b d) -> p b d", d=P),
                          Wd.rearrange("e f d -> (e f) d").rearrange("(b p) d -> p b d", p=P)).then_inc(s_w["d"], 16)

            def split_hi(names):
                for name, cols in WCOLS:
                    if name in names:
                        act.wait_ge(s_w[name], 32 if name == "s" else 16)
                        nc.scalar.activation(w_hi[:, off[name]:off[name] + cols], view(name, cols), ACT.Copy)\
                          .then_inc(s_hi_w, 1)

            def x_hi(ch):
                act.wait_ge(s_xT, ch.n(1, 1))
                nc.scalar.activation(xT_hi[:, ch.par], p_front[:, :], ACT.Copy).then_inc(s_xhi, 1)

            def rec_in(ch, j):
                par = slot_par(ch, j)
                act.wait_ge(s_gate, ch.n(SLOTS, j + 1))
                nc.scalar.activation(rec_z[:, j], p_gate[par][:, :], ACT.Tanh, scale=0.5).then_inc(s_tanh, 1)
                act.wait_ge(s_lin, ch.n(SLOTS, j + 1))
                nc.scalar.activation(rec_v[:, j], p_lin[par][:, :], ACT.Relu).then_inc(s_relu, 1)
                act.wait_ge(s_tanh, ch.n(NH, j + 1))
                nc.scalar.activation(rec_z[:, j], rec_z[:, j], ACT.Identity, bias=consts[:, 2:3], scale=0.5)\
                  .then_inc(s_z, 1)

            def rec_hi(ch, j):
                act.wait_ge(s_scan, ch.n(NH, j + 1))
                nc.scalar.activation(act_hi[:, j], rec_h[:, j], ACT.Copy).then_inc(s_hhi, 1)

            def silu(ch, k, c):
                f, par = k - NH, slot_par(ch, k)
                act.wait_ge(s_gate, ch.n(SLOTS, k + 1))
                if f >= 2:
                    act.wait_ge(s_p, ch.n(NF, f - 1))
                elif f + NF - 2 >= 0 and has(c, -1):
                    act.wait_ge(s_p, ch.at(-1).n(NF, NF))
                nc.scalar.activation(silu_g[:, par], p_gate[par][:, :], ACT.Silu).then_inc(s_silu, 1)

            def ffn_hi(ch, k):
                f = k - NH
                if f == 0:
                    act.wait_ge(s_p, ch.n(NF, 1))
                else:
                    act.wait_ge(s_q, ch.n(NB, f))
                nc.scalar.activation(act_hi[:, k], prod[:, f], ACT.Copy).then_inc(s_fhi, 1)

            def copy_lgT(ch):
                act.wait_ge(s_rl, ch.n(1, 1))
                nc.scalar.activation(lgT[:, :], p_front[0:2 * E, :], ACT.Copy).then_inc(s_lgT, 1)

            def router_silus(ch):
                act.wait_ge(s_shift, ch.n(1, 1))
                nc.scalar.activation(silu_n[:, :, :], shifted[:, :, :], ACT.Silu, bias=consts[:, 0:1])
                nc.scalar.activation(silu_p[:, :, :], shifted[:, :, :], ACT.Silu, bias=consts[:, 1:2], scale=-1.0)\
                  .then_inc(s_rsil, 1)

            def copy_cwT(ch, reused):
                act.wait_ge(s_cwTp, ch.n(1, 1))
                if reused:
                    act.wait_ge(s_cws, ch.at(-1).n(16, 16))
                nc.scalar.activation(cwT[:, :], p_front[0:E * TT, 0:P], ACT.Copy).then_inc(s_cwT, 1)

            def ffn_silu(ch):
                act.wait_ge(s_down, ch.n(NF, NF))
                nc.scalar.activation(ffn_gate[:, :], p_ffn[:, :], ACT.Silu).then_inc(s_gsil, 1)

            act.wait_ge(s_const, CONSTS)
            nc.scalar.activation(silu_n[:, 0, 0:3], consts[:, :], ACT.Silu)
            split_hi(("r", "hg"))
            first = Chunk(0, 0)
            x_hi(first)
            split_hi(("s", "g", "u"))
            copy_lgT(first)
            router_silus(first)
            split_hi(("o", "sd", "d"))
            copy_cwT(first, False)

            def chunk(ch, c):
                for k in range(SLOTS):
                    if k == 0 and has(c, 1):
                        x_hi(ch.at(1))
                    if k == 2 and has(c, 1):
                        copy_lgT(ch.at(1))
                    if k == 3 and has(c, -1):
                        ffn_silu(ch.at(-1))
                    if k == 5 and has(c, 1):
                        router_silus(ch.at(1))
                    if k < NH:
                        rec_in(ch, k)
                    else:
                        silu(ch, k, c)
                    if k == 9 and has(c, 1):
                        copy_cwT(ch.at(1), True)
                    if k == 0 and has(c, -1):
                        ffn_hi(ch.at(-1), SLOTS - 1)
                    if k in (2, 3):
                        rec_hi(ch, k - 2)
                    if k > NH:
                        ffn_hi(ch, k - 1)

            chunks(act, chunk)
            last = Chunk(NCH // 2 - 1, 1)
            ffn_hi(last, SLOTS - 1)
            ffn_silu(last)

        @block.vector
        def _(dve):
            def ln_stats(ch):
                dve.wait_ge(s_xin[ch.par], ch.dma())
                for t in range(TT):
                    last = nc.vector.bn_stats(stats[:, t], x_in[:, ch.par, t])
                last.then_inc(s_stat, 1)

            def ln_stats_landed(ch):
                dve.wait_ge(s_stat, ch.n(1, 1))

            def ln_mean_var(ch):
                for t in range(TT):
                    last = nc.vector.bn_aggr(meanvar[:, t], stats[:, t])
                last.then_inc(s_mv, 1)

            def normalise(ch, reused):
                dve.wait_ge(s_rstd, ch.n(1, 1))
                if reused:
                    dve.wait_ge(s_xT, ch.at(-1).n(1, 1))
                for t in range(TT):
                    last = nc.vector.tensor_scalar(xn[:, t], x_in[:, ch.par, t], meanvar[:, t, 0:1], rstd[:, t:t + 1],
                                                   ALU.subtract, ALU.mult)
                last.then_inc(s_norm, 1)

            def x_lo(ch):
                dve.wait_ge(s_xhi, ch.n(1, 1))
                nc.vector.tensor_tensor(xT_lo[:, ch.par], p_front[:, :], xT_hi[:, ch.par].bitcast(F32), ALU.subtract)\
                  .then_inc(s_xlo, 1)

            def split_lo(names):
                for n, (name, cols) in enumerate(WCOLS):
                    if name in names:
                        w = slice(off[name], off[name] + cols)
                        dve.wait_ge(s_hi_w, n + 1)
                        nc.vector.tensor_tensor(w_lo[:, w], stage[:, w], w_hi[:, w].bitcast(F32), ALU.subtract)\
                          .then_inc(s_lo_w, 1)

            def rec_scan(ch, j):
                dve.wait_ge(s_a, ch.n(NH, j + 1))
                dve.wait_ge(s_relu, ch.n(NH, j + 1))
                nc.vector.scalar_tensor_tensor(out=rec_v[:, j], in0=rec_v[:, j], scalar=0.5, in1=rec_z[:, j],
                                               op0=ALU.add, op1=ALU.mult).then_inc(s_v, 1)
                dve.wait_ge(s_v, ch.n(NH, j + 1))
                for q in range(SEQS):
                    w = slice(q * S, (q + 1) * S)
                    last = nc.vector.tensor_tensor_scan(rec_h[:, j, w], rec_a[:, j, w], rec_v[:, j, w], 0.0,
                                                        ALU.mult, ALU.add)
                last.then_inc(s_scan, 1)

            def gated(ch, k):
                f, par = k - NH, slot_par(ch, k)
                dve.wait_ge(s_silu, ch.n(NF, f + 1))
                dve.wait_ge(s_lin, ch.n(SLOTS, k + 1))
                nc.vector.tensor_tensor(prod[:, f], p_lin[par][:, :], silu_g[:, par], ALU.mult).then_inc(s_p, 1)
                if f:
                    if f == 1:
                        dve.wait_ge(s_cwa[ch.par], ch.dma(2))
                    if f == 1 + NB // 2:
                        dve.wait_ge(s_cwb[ch.par], ch.dma(2))
                    dve.wait_ge(s_p, ch.n(NF, f + 1))
                    nc.vector.tensor_tensor(prod[:, f], prod[:, f], cw[:, ch.par, f - 1], ALU.mult).then_inc(s_q, 1)

            def step(ch, n, ins):
                ins.then_inc(s_rt, 1)
                dve.wait_ge(s_rt, ch.n(ROUTER_STEPS, n))

            def router_sum(ch):
                dve.wait_ge(s_lt, ch.n(1, 1))
                both = p_front[:, 0:TT * 2 * E].rearrange("p (t h e) -> p t e h", t=TT, h=2)
                step(ch, 1, nc.vector.tensor_reduce(lg[:, :, :], both, AX.X, ALU.add))

            def router_max(ch):
                for t in range(TT):
                    last = nc.vector.max(top8[:, t], lg[:, t])
                step(ch, 2, last)

            def router_index(ch):
                nc.vector.tensor_tensor(shifted[:, :, :], lg[:, :, :], top8[:, :, 0:1].to_broadcast([P, TT, E]),
                                        ALU.subtract).then_inc(s_shift, 1)
                for t in range(TT):
                    last = nc.vector.max_index(top8_at[:, t], top8[:, t], lg[:, t])
                step(ch, 3, last)

            def router_exp(ch):
                dve.wait_ge(s_rsil, ch.n(1, 1))
                step(ch, 4, nc.vector.reciprocal(expv[:, :, :], silu_p[:, :, :]))
                step(ch, 5, nc.vector.scalar_tensor_tensor(out=expv[:, :, :], in0=silu_n[:, :, :], scalar=-1.0,
                                                           in1=expv[:, :, :], op0=ALU.mult, op1=ALU.mult))
                step(ch, 6, nc.vector.tensor_reduce(esum[:, :], expv[:, :, :], AX.X, ALU.add))
                nc.vector.reciprocal(rsum[:, :], esum[:, :]).then_inc(s_rt, 1)

            def router_weights(ch):
                at0, at1 = (top8_at[:, :, n:n + 1].to_broadcast([P, TT, E]) for n in range(2))
                experts = iota_e[:, :].rearrange("p (t e) -> p t e", t=1).to_broadcast([P, TT, E])
                nc.vector.tensor_tensor(mask0[:, :, :], experts, at0, ALU.is_equal)
                nc.vector.tensor_tensor(mask1[:, :, :], experts, at1, ALU.is_equal).then_inc(s_rt, 1)
                dve.wait_ge(s_rt, ch.n(ROUTER_STEPS, 8))
                step(ch, 9, nc.vector.tensor_tensor(mask0[:, :, :], mask0[:, :, :], mask1[:, :, :], ALU.add))
                step(ch, 10, nc.vector.tensor_tensor(mask0[:, :, :], mask0[:, :, :], expv[:, :, :], ALU.mult))
                nc.vector.tensor_tensor(cw_tok[:, :, :].rearrange("p e t -> p t e"), mask0[:, :, :],
                                        rsum[:, :].rearrange("p (t e) -> p t e", e=1).to_broadcast([P, TT, E]),
                                        ALU.mult).then_inc(s_cwtok, 1)

            def gate_out(ch):
                dve.wait_ge(s_gsil, ch.n(1, 1))
                dve.wait_ge(s_rec, ch.n(1, 1))
                nc.vector.tensor_tensor(sg[:, :], p_rec[:, :], ffn_gate[:, :], ALU.mult).then_inc(s_sg, 1)

            def add_out(ch):
                dve.wait_ge(s_ot, ch.n(1, 1))
                dve.wait_ge(s_xres[ch.par], ch.dma())
                res = x_out[:, ch.par].rearrange("p t d -> p (t d)")
                nc.vector.tensor_tensor(res, p_out[:, :], res, ALU.add).then_inc(s_add, 1)

            first, second = Chunk(0, 0), Chunk(0, 1)
            ln_stats(first)
            ln_stats_landed(first)
            ln_mean_var(first)
            dve.wait_ge(s_const, CONSTS)
            normalise(first, False)
            split_lo(("r",))
            dve.wait_ge(s_lo_w, 1)
            nc.vector.tensor_copy(wr_both[:, 0:E], w_hi[:, 0:E].bitcast(F32))
            nc.vector.tensor_copy(wr_both[:, E:2 * E], w_lo[:, 0:E].bitcast(F32)).then_inc(s_lo_w, 1)
            split_lo(("hg",))
            x_lo(first)
            ln_stats(second)
            ln_stats_landed(second)
            ln_mean_var(second)
            split_lo(("s",))
            router_sum(first)
            router_max(first)
            router_index(first)
            normalise(second, True)
            split_lo(("g",))
            router_exp(first)
            router_weights(first)
            split_lo(("u", "o", "sd", "d"))

            def chunk(ch, c):
                for k in range(SLOTS):
                    if k == 0 and has(c, 1):
                        x_lo(ch.at(1))
                    if k in (1, 2):
                        rec_scan(ch, k - 1)
                    if k == 4 and has(c, -1):
                        gate_out(ch.at(-1))
                    if k == 6 and has(c, -1):
                        add_out(ch.at(-1))
                    if k == 10 and has(c, 2):
                        normalise(ch.at(2), True)
                    if k == 3 and has(c, 1):
                        router_sum(ch.at(1))
                    if k == 9 and has(c, 2):
                        ln_stats_landed(ch.at(2))
                    if k >= NH:
                        gated(ch, k)
                    if k == 3 and has(c, 1):
                        router_max(ch.at(1))
                    if k == 9 and has(c, 2):
                        ln_mean_var(ch.at(2))
                    if k == 4 and has(c, 1):
                        router_index(ch.at(1))
                    if k == 6 and has(c, 1):
                        router_exp(ch.at(1))
                    if k == 7 and has(c, 1):
                        router_weights(ch.at(1))
                    if k == 8 and has(c, 2):
                        ln_stats(ch.at(2))

            chunks(dve, chunk)
            last = Chunk(NCH // 2 - 1, 1)
            gate_out(last)
            add_out(last)

        @block.tensor
        def _(pe):
            split_count = {}
            for n, (name, _) in enumerate(WCOLS):
                split_count[name] = n + 1 + (n > 0)

            def split_product(acc, name, col, hi, lo, start, stop):
                w = slice(off[name] + col * P, off[name] + (col + 1) * P)
                nc.tensor.matmul(acc, w_hi[:, w], hi, start=start, stop=False)
                nc.tensor.matmul(acc, w_hi[:, w], lo, start=False, stop=False)
                return nc.tensor.matmul(acc, w_lo[:, w], hi, start=False, stop=stop)

            def transpose_x(ch, reused):
                pe.wait_ge(s_norm, ch.n(1, 1))
                if reused:
                    pe.wait_ge(s_cwT, ch.at(-1).n(1, 1))
                for t in range(TT):
                    last = nc.tensor.transpose(p_front[:, t * P:(t + 1) * P], xn[:, t], ident[:, :])
                last.then_inc(s_xT, 1)

            def router_logits(ch):
                pe.wait_ge(s_xlo, ch.n(1, 1))
                nc.tensor.matmul(p_front[0:2 * E, :], wr_both[:, :], xT_hi[:, ch.par], start=True, stop=False)
                nc.tensor.matmul(p_front[0:2 * E, :], wr_both[:, :], xT_lo[:, ch.par], start=False, stop=True)\
                  .then_inc(s_rl, 1)

            def transpose_logits(ch):
                pe.wait_ge(s_const, CONSTS)
                pe.wait_ge(s_lgT, ch.n(1, 1))
                for t in range(TT):
                    last = nc.tensor.transpose(p_front[:, t * 2 * E:(t + 1) * 2 * E], lgT[:, t * P:(t + 1) * P],
                                               ident[0:2 * E, 0:2 * E])
                last.then_inc(s_lt, 1)

            def transpose_cw(ch):
                pe.wait_ge(s_const, CONSTS)
                pe.wait_ge(s_cwtok, ch.n(1, 1))
                nc.tensor.transpose(p_front[0:E * TT, 0:P], cw_tok[:, :, :].rearrange("p e t -> p (e t)"),
                                    ident[:, :]).then_inc(s_cwTp, 1)

            def up(ch, k, c):
                par = slot_par(ch, k)
                hi, lo = xT_hi[:, ch.par], xT_lo[:, ch.par]
                former, fk = (ch, k - 2) if k >= 2 else (ch.at(-1), k - 2 + SLOTS)
                known = k >= 2 or has(c, -1)
                if k < NH:
                    gate, lin = ("hg", NH + k), ("hg", k)
                elif k == NH:
                    gate, lin = ("s", 0), ("s", 1)
                else:
                    gate, lin = ("g", k - NH - 1), ("u", k - NH - 1)
                if c == 0:
                    pe.wait_ge(s_lo_w, split_count[lin[0]])
                if known and fk < NH:
                    pe.wait_ge(s_tanh, former.n(NH, fk + 1))
                elif known:
                    pe.wait_ge(s_silu, former.n(NF, fk - NH + 1))
                split_product(p_gate[par][:, :], *gate, hi, lo, True, True).then_inc(s_gate, 1)
                if known and fk < NH:
                    pe.wait_ge(s_relu, former.n(NH, fk + 1))
                elif known:
                    pe.wait_ge(s_p, former.n(NF, fk - NH + 1))
                split_product(p_lin[par][:, :], *lin, hi, lo, True, True).then_inc(s_lin, 1)

            def down(ch, k, c):
                f = k - NH
                if f == 0 and c == 0:
                    pe.wait_ge(s_lo_w, split_count["d"])
                if f == 0 and has(c, -1):
                    pe.wait_ge(s_gsil, ch.at(-1).n(1, 1))
                pe.wait_ge(s_flo, ch.n(NF, f + 1))
                split_product(p_ffn[:, :], "sd" if f == 0 else "d", max(f - 1, 0), act_hi[:, k], act_lo[:, k],
                              f == 0, f == NF - 1).then_inc(s_down, 1)

            def rec_down(ch, j, c):
                if j == 0 and has(c, -1):
                    pe.wait_ge(s_sg, ch.at(-1).n(1, 1))
                pe.wait_ge(s_hlo, ch.n(NH, j + 1))
                last = split_product(p_rec[:, :], "o", j, act_hi[:, j], act_lo[:, j], j == 0, j == NH - 1)
                if j == NH - 1:
                    last.then_inc(s_rec, 1)

            def transpose_out(ch, reused):
                pe.wait_ge(s_sg, ch.n(1, 1))
                if reused:
                    pe.wait_ge(s_add, ch.at(-1).n(1, 1))
                for t in range(TT):
                    last = nc.tensor.transpose(p_out[:, t * P:(t + 1) * P], sg[:, t * P:(t + 1) * P], ident[:, :])
                last.then_inc(s_ot, 1)

            first = Chunk(0, 0)
            pe.wait_ge(s_const, CONSTS)
            transpose_x(first, False)
            pe.wait_ge(s_lo_w, 2)
            router_logits(first)
            transpose_logits(first)
            transpose_cw(first)

            def chunk(ch, c):
                for k in range(SLOTS):
                    if k == 0 and has(c, 1):
                        transpose_x(ch.at(1), True)
                    up(ch, k, c)
                    if k == 1 and has(c, 1):
                        router_logits(ch.at(1))
                    if k == 2 and has(c, 1):
                        transpose_logits(ch.at(1))
                    if k < LAG and has(c, -1):
                        down(ch.at(-1), k - LAG + SLOTS, None)
                    if k == 5 and has(c, -1):
                        transpose_out(ch.at(-1), has(c, -2))
                    if k - LAG >= NH:
                        down(ch, k - LAG, c)
                    if k in (5, 6):
                        rec_down(ch, k - 5, c)
                    if k == 8 and has(c, 1):
                        transpose_cw(ch.at(1))

            chunks(pe, chunk)
            last = Chunk(NCH // 2 - 1, 1)
            for k in range(SLOTS - LAG, SLOTS):
                down(last, k, None)
            transpose_out(last, True)


_INS = ["L0_attn_x", "L0_attn_W_hg", "L0_attn_W_out", "L0_ffn_Wr", "L0_ffn_Wg", "L0_ffn_Wu", "L0_ffn_Wd",
        "L0_ffn_Sg", "L0_ffn_Su", "L0_ffn_Sd"]


def kernel(**inputs):
    import numpy as _np
    import concourse.bacc as _bacc
    from concourse import mybir as _mybir
    from concourse.bass_utils import run_bass_kernel_spmd as _run

    nc = _bacc.Bacc("TRN2", target_bir_lowering=False, num_devices=1)
    arrays, args = {}, []
    for name in _INS:
        a = _np.ascontiguousarray(inputs[name])
        arrays[f"in_{name}"] = a
        args.append(nc.dram_tensor(f"in_{name}", a.shape, _mybir.dt.from_np(a.dtype), kind="ExternalInput").ap())
    shape = arrays["in_L0_attn_x"].shape
    result = nc.dram_tensor("out_x", shape, _mybir.dt.float32, kind="ExternalOutput").ap()
    recurrent_moe_block(nc, *args, result)
    r = _run(nc, [arrays], core_ids=[0])
    return r.results[0]["out_x"]
```

```python
from contextlib import ExitStack

import concourse.bass as bass
from concourse import mybir

F32 = mybir.dt.float32
F32R = mybir.dt.float32r
U32 = mybir.dt.uint32
ALU = mybir.AluOpType
ACT = mybir.ActivationFunctionType
AX = mybir.AxisListType

P = 128
CT = 512
TT = CT // P
NH = 2
NF = 9
SLOTS = NH + NF
LAG = 3


class Chunk:

    def __init__(self, i, par):
        self.i, self.par = i, par

    def at(self, d):
        return Chunk(self.i + (self.par + d) // 2, (self.par + d) % 2)

    def n(self, per, k=0):
        return self.i * (2 * per) + (self.par * per + k)

    def dma(self, times=1):
        return self.i * (16 * times) + 16 * times


def recurrent_moe_block(nc, x, W_hg, W_out, Wr, Wg, Wu, Wd, Sg, Su, Sd, out):
    B, S, D = x.shape
    E, _, F = Wg.shape
    T = B * S
    NCH = T // CT
    NB = E * F // P
    SEQS = CT // S
    assert D == P and NB + 1 == NF and NCH % 2 == 0 and NCH >= 4 and CT % S == 0

    x_tiles = x.rearrange("b s d -> (b s) d").rearrange("(c t p) d -> c p t d", p=P, t=TT)
    out_tiles = out.rearrange("b s d -> (b s) d").rearrange("(c t p) d -> c p t d", p=P, t=TT)
    cw_dram = nc.dram_tensor("cw_scratch", (2, E, CT), F32, kind="Internal").ap()

    with ExitStack() as ctx:
        def sb(name, shape, dt=F32):
            return ctx.enter_context(nc.sbuf_tensor(name, shape, dt))

        def sem(name):
            return ctx.enter_context(nc.semaphore(name))

        def sem2(name):
            return [sem(f"{name}{k}") for k in range(2)]

        WCOLS = [("r", E), ("hg", 4 * P), ("s", 2 * P), ("g", NB * P), ("u", NB * P),
                 ("o", NH * P), ("sd", P), ("d", NB * P)]
        off, at = {}, 0
        for name, cols in WCOLS:
            off[name] = at
            at += cols
        w_hi = sb("w_hi", [P, at], F32R)
        w_lo = sb("w_lo", [P, at], F32R)
        wr_both = sb("wr_both", [P, 2 * E], F32R)
        ident = sb("ident", [P, P])
        iota_e = sb("iota_e", [P, E])
        consts = sb("consts", [P, 3])
        eps = sb("eps", [P, TT])
        minus_half = sb("minus_half", [P, TT])

        x_in = sb("x_in", [P, 2, TT, P])
        x_out = sb("x_out", [P, 2, TT, P])
        xn = sb("xn", [P, TT, P])
        stats = sb("stats", [P, TT, 6])
        meanvar = sb("meanvar", [P, TT, 2])
        var_eps = sb("var_eps", [P, TT])
        rstd = sb("rstd", [P, TT])
        xT_hi = sb("xT_hi", [P, 2, CT], F32R)
        xT_lo = sb("xT_lo", [P, 2, CT], F32R)
        rec_z = sb("rec_z", [P, NH, CT])
        rec_a = sb("rec_a", [P, NH, CT])
        rec_v = sb("rec_v", [P, NH, CT])
        rec_h = sb("rec_h", [P, NH, CT])
        silu_g = sb("silu_g", [P, 2, CT])
        prod = sb("prod", [P, NF, CT])
        act_hi = sb("act_hi", [P, SLOTS, CT], F32R)
        act_lo = sb("act_lo", [P, SLOTS, CT], F32R)
        lgT = sb("lgT", [2 * E, CT])
        lg = sb("lg", [P, TT, E])
        top8 = sb("top8", [P, TT, 8])
        top8_at = sb("top8_at", [P, TT, 8], U32)
        shifted = sb("shifted", [P, TT, E])
        silu_n = sb("silu_n", [P, TT, E])
        silu_p = sb("silu_p", [P, TT, E])
        expv = sb("expv", [P, TT, E])
        esum = sb("esum", [P, TT])
        rsum = sb("rsum", [P, TT])
        mask0 = sb("mask0", [P, TT, E])
        mask1 = sb("mask1", [P, TT, E])
        cw_tok = sb("cw_tok", [P, P // TT, TT])
        cwT = sb("cwT", [E * TT, P])
        cw = sb("cw", [P, 2, NB, CT])
        ffn_gate = sb("ffn_gate", [P, CT])
        sg = sb("sg", [P, CT])
        stage = prod[:, :, :].rearrange("p k n -> p (k n)")
        assert at <= NF * CT

        psum = lambda name: ctx.enter_context(nc.psum_tensor(name, [P, CT], F32))
        p_gate = [psum("p_gate0"), psum("p_gate1")]
        p_lin = [psum("p_lin0"), psum("p_lin1")]
        p_ffn = psum("p_ffn")
        p_rec = psum("p_rec")
        p_front = psum("p_front")
        p_out = psum("p_out")

        s_w = {name: sem(f"w_landed_{name}") for name, _ in WCOLS}
        s_hi_w, s_lo_w = sem("weights_hi"), sem("weights_lo")
        s_const0, s_const = sem("ident_zeroed"), sem("constants_ready")
        s_xin, s_xres, s_stored = sem2("x_landed"), sem2("residual_landed"), sem2("out_stored")
        s_cws, s_cwa, s_cwb = sem("cw_stored"), sem2("cw_first_half"), sem2("cw_second_half")
        s_stat, s_mv, s_ve, s_rstd, s_norm = (sem("bn_stats_done"), sem("mean_var_ready"), sem("var_eps_ready"),
                                              sem("rstd_ready"), sem("normalised"))
        s_xT, s_xhi, s_xlo = sem("xT_in_psum"), sem("xT_hi_ready"), sem("xT_lo_ready")
        s_rl, s_lgT, s_lt = sem("router_logits_T"), sem("logits_T_copied"), sem("router_logits")
        s_rt, s_shift, s_rsil, s_cwtok = sem("router_step"), sem("logits_shifted"), sem("router_silus"), sem("cw_ready")
        s_cwTp, s_cwT = sem("cwT_in_psum"), sem("cwT_copied")
        s_gate, s_lin = sem("gate_in_psum"), sem("linear_in_psum")
        s_tanh, s_relu, s_z, s_a, s_v, s_scan = (sem("tanh_done"), sem("relu_done"), sem("z_done"), sem("a_done"), sem("v_done"),
                                             sem("scan_done"))
        s_hhi, s_hlo = sem("rec_hi_ready"), sem("rec_lo_ready")
        s_silu, s_p, s_q = sem("silu_done"), sem("gated_done"), sem("weighted_done")
        s_fhi, s_flo, s_down = sem("ffn_hi_ready"), sem("ffn_lo_ready"), sem("down_done")
        s_rec, s_gsil, s_sg, s_ot, s_add = (sem("rec_out_done"), sem("ffn_gate_done"), sem("sg_done"),
                                            sem("out_in_psum"), sem("out_added"))
        block = ctx.enter_context(nc.Block())

        CONSTS = 8
        ROUTER_STEPS = 9

        def chunks(engine, chunk, end=None):
            chunk(Chunk(0, 0), 0)
            chunk(Chunk(0, 1), 1)
            with engine.Fori(1, NCH // 2 - 1) as i:
                chunk(Chunk(i, 0), None)
                chunk(Chunk(i, 1), None)
            chunk(Chunk(NCH // 2 - 1, 0), NCH - 2)
            chunk(Chunk(NCH // 2 - 1, 1), NCH - 1)

        def has(c, d):
            return c is None or 0 <= c + d < NCH

        def slot_par(ch, k):
            return (SLOTS * ch.par + k) % 2

        @block.sync
        def _(sp):
            def load_x(ch):
                if isinstance(ch.i, int) and ch.i == 0:
                    pass
                else:
                    sp.wait_ge(s_norm, ch.at(-2).n(1, 1))
                c = ch.i * 2 + ch.par
                sp.dma_start(x_in[:, ch.par], x_tiles[c]).then_inc(s_xin[ch.par], 16)

            load_x(Chunk(0, 0))
            load_x(Chunk(0, 1))

            def chunk(ch, c):
                if has(c, 2):
                    load_x(ch.at(2))
                if has(c, -2):
                    sp.wait_ge(s_stored[ch.par], ch.at(-2).dma())
                sp.dma_start(x_out[:, ch.par], x_tiles[ch.i * 2 + ch.par]).then_inc(s_xres[ch.par], 16)
                if has(c, -1):
                    store(ch.at(-1))
                if has(c, 1):
                    spread(ch.at(1), has(c, -1))

            def store(ch):
                sp.wait_ge(s_add, ch.n(1, 1))
                sp.dma_start(out_tiles[ch.i * 2 + ch.par], x_out[:, ch.par]).then_inc(s_stored[ch.par], 16)

            def spread(ch, reused):
                sp.wait_ge(s_cwT, ch.n(1, 1))
                if reused:
                    sp.wait_ge(s_cwb[ch.par], ch.at(-2).dma(2))
                sp.dma_start(cw_dram[ch.par].rearrange("e (t n) -> (e t) n", t=TT), cwT[:, :]).then_inc(s_cws, 16)
                sp.wait_ge(s_cws, ch.n(16, 16))
                if reused:
                    sp.wait_ge(s_q, ch.at(-2).n(NB, NB))
                for half, landed in ((0, s_cwa), (1, s_cwb)):
                    b0, b1 = half * NB // 2, (half + 1) * NB // 2
                    for e in range(2):
                        rows = cw_dram[ch.par, 2 * b0 + e:2 * b1:2, :]
                        spread_rows = bass.AP(tensor=rows.tensor, offset=rows.offset,
                                              ap=[[0, F]] + [list(d) for d in rows.ap])
                        sp.dma_start(cw[e * F:(e + 1) * F, ch.par, b0:b1, :], spread_rows)\
                          .then_inc(landed[ch.par], 16)

            spread(Chunk(0, 0), False)
            chunks(sp, chunk)
            last = Chunk(NCH // 2 - 1, 1)
            store(last)
            sp.wait_ge(s_stored[0], last.at(-1).dma())
            sp.wait_ge(s_stored[1], last.dma())
            sp.wait_ge(s_cws, last.n(16, 16))

        @block.gpsimd
        def _(pool):
            nc.gpsimd.memset(minus_half[:, :], -0.5).then_inc(s_const, 1)
            nc.gpsimd.memset(ident[:, :], 0.0).then_inc(s_const0, 1)
            pool.wait_ge(s_const0, 1)
            nc.gpsimd.affine_select(out=ident[:, :], in_=ident[:, :], compare_op=ALU.not_equal, fill=1.0, base=0,
                                    pattern=[[-1, P]], channel_multiplier=1).then_inc(s_const, 1)
            nc.gpsimd.iota(iota_e[:, :], [[1, E]], base=0, channel_multiplier=0,
                           allow_small_or_imprecise_dtypes=True).then_inc(s_const, 1)
            for col, value in enumerate((-1.0, 1.0, 0.5)):
                nc.gpsimd.memset(consts[:, col:col + 1], value).then_inc(s_const, 1)
            nc.gpsimd.memset(eps[:, :], 1e-5).then_inc(s_const, 1)
            nc.gpsimd.memset(cw_tok[:, E:, :], 0.0).then_inc(s_const, 1)
            pool.wait_ge(s_const, CONSTS)

            def rstd_of(ch):
                pool.wait_ge(s_mv, ch.n(1, 1))
                nc.gpsimd.tensor_tensor(var_eps[:, :], meanvar[:, :, 1], eps[:, :], ALU.add).then_inc(s_ve, 1)
                pool.wait_ge(s_ve, ch.n(1, 1))
                nc.gpsimd.tensor_tensor(rstd[:, :], var_eps[:, :], minus_half[:, :], ALU.pow).then_inc(s_rstd, 1)

            def decay(ch, j):
                pool.wait_ge(s_z, ch.n(NH, j + 1))
                nc.gpsimd.tensor_tensor(rec_a[:, j], consts[:, 1:2].to_broadcast([P, CT]), rec_z[:, j], ALU.subtract)\
                  .then_inc(s_a, 1)

            def rec_lo(ch, j):
                pool.wait_ge(s_hhi, ch.n(NH, j + 1))
                nc.gpsimd.tensor_tensor(act_lo[:, j], rec_h[:, j], act_hi[:, j].bitcast(F32), ALU.subtract)\
                  .then_inc(s_hlo, 1)

            def ffn_lo(ch, k):
                f = k - NH
                pool.wait_ge(s_fhi, ch.n(NF, f + 1))
                nc.gpsimd.tensor_tensor(act_lo[:, k], prod[:, f], act_hi[:, k].bitcast(F32), ALU.subtract)\
                  .then_inc(s_flo, 1)

            rstd_of(Chunk(0, 0))
            rstd_of(Chunk(0, 1))

            def chunk(ch, c):
                for k in range(SLOTS):
                    if k < NH:
                        decay(ch, k)
                    if k == 0 and has(c, -1):
                        ffn_lo(ch.at(-1), SLOTS - 1)
                    if k in (2, 3):
                        rec_lo(ch, k - 2)
                    if k > NH:
                        ffn_lo(ch, k - 1)
                    if k == 5 and has(c, 2):
                        rstd_of(ch.at(2))

            chunks(pool, chunk)
            ffn_lo(Chunk(NCH // 2 - 1, 1), SLOTS - 1)

        @block.scalar
        def _(act):
            def view(name, n):
                return stage[:, off[name]:off[name] + n]

            act.dma_start(view("r", E), Wr).then_inc(s_w["r"], 16)
            act.dma_start(view("hg", 4 * P), W_hg).then_inc(s_w["hg"], 16)
            act.dma_start(view("s", P), Sg).then_inc(s_w["s"], 16)
            act.dma_start(stage[:, off["s"] + P:off["s"] + 2 * P], Su).then_inc(s_w["s"], 16)
            act.dma_start(view("g", NB * P).rearrange("p (e f) -> p e f", f=F),
                          Wg.rearrange("e d f -> d e f")).then_inc(s_w["g"], 16)
            act.dma_start(view("u", NB * P).rearrange("p (e f) -> p e f", f=F),
                          Wu.rearrange("e d f -> d e f")).then_inc(s_w["u"], 16)
            act.dma_start(view("o", NH * P).rearrange("p (b d) -> p b d", d=P),
                          W_out.rearrange("(b p) d -> p b d", p=P)).then_inc(s_w["o"], 16)
            act.dma_start(view("sd", P), Sd).then_inc(s_w["sd"], 16)
            act.dma_start(view("d", NB * P).rearrange("p (b d) -> p b d", d=P),
                          Wd.rearrange("e f d -> (e f) d").rearrange("(b p) d -> p b d", p=P)).then_inc(s_w["d"], 16)

            def split_hi(names):
                for name, cols in WCOLS:
                    if name in names:
                        act.wait_ge(s_w[name], 32 if name == "s" else 16)
                        nc.scalar.activation(w_hi[:, off[name]:off[name] + cols], view(name, cols), ACT.Copy)\
                          .then_inc(s_hi_w, 1)

            def x_hi(ch):
                act.wait_ge(s_xT, ch.n(1, 1))
                nc.scalar.activation(xT_hi[:, ch.par], p_front[:, :], ACT.Copy).then_inc(s_xhi, 1)

            def rec_in(ch, j):
                par = slot_par(ch, j)
                act.wait_ge(s_gate, ch.n(SLOTS, j + 1))
                nc.scalar.activation(rec_z[:, j], p_gate[par][:, :], ACT.Tanh, scale=0.5).then_inc(s_tanh, 1)
                act.wait_ge(s_lin, ch.n(SLOTS, j + 1))
                nc.scalar.activation(rec_v[:, j], p_lin[par][:, :], ACT.Relu).then_inc(s_relu, 1)
                act.wait_ge(s_tanh, ch.n(NH, j + 1))
                nc.scalar.activation(rec_z[:, j], rec_z[:, j], ACT.Identity, bias=consts[:, 2:3], scale=0.5)\
                  .then_inc(s_z, 1)

            def rec_hi(ch, j):
                act.wait_ge(s_scan, ch.n(NH, j + 1))
                nc.scalar.activation(act_hi[:, j], rec_h[:, j], ACT.Copy).then_inc(s_hhi, 1)

            def silu(ch, k, c):
                f, par = k - NH, slot_par(ch, k)
                act.wait_ge(s_gate, ch.n(SLOTS, k + 1))
                if f >= 2:
                    act.wait_ge(s_p, ch.n(NF, f - 1))
                elif f + NF - 2 >= 0 and has(c, -1):
                    act.wait_ge(s_p, ch.at(-1).n(NF, NF))
                nc.scalar.activation(silu_g[:, par], p_gate[par][:, :], ACT.Silu).then_inc(s_silu, 1)

            def ffn_hi(ch, k):
                f = k - NH
                if f == 0:
                    act.wait_ge(s_p, ch.n(NF, 1))
                else:
                    act.wait_ge(s_q, ch.n(NB, f))
                nc.scalar.activation(act_hi[:, k], prod[:, f], ACT.Copy).then_inc(s_fhi, 1)

            def copy_lgT(ch):
                act.wait_ge(s_rl, ch.n(1, 1))
                nc.scalar.activation(lgT[:, :], p_front[0:2 * E, :], ACT.Copy).then_inc(s_lgT, 1)

            def router_silus(ch):
                act.wait_ge(s_shift, ch.n(1, 1))
                nc.scalar.activation(silu_n[:, :, :], shifted[:, :, :], ACT.Silu, bias=consts[:, 0:1])
                nc.scalar.activation(silu_p[:, :, :], shifted[:, :, :], ACT.Silu, bias=consts[:, 1:2], scale=-1.0)\
                  .then_inc(s_rsil, 1)

            def copy_cwT(ch, reused):
                act.wait_ge(s_cwTp, ch.n(1, 1))
                if reused:
                    act.wait_ge(s_cws, ch.at(-1).n(16, 16))
                nc.scalar.activation(cwT[:, :], p_out[0:E * TT, 0:P], ACT.Copy).then_inc(s_cwT, 1)

            def ffn_silu(ch):
                act.wait_ge(s_down, ch.n(NF, NF))
                nc.scalar.activation(ffn_gate[:, :], p_ffn[:, :], ACT.Silu).then_inc(s_gsil, 1)

            act.wait_ge(s_const, CONSTS)
            nc.scalar.activation(silu_n[:, 0, 0:3], consts[:, :], ACT.Silu)
            split_hi(("r", "hg"))
            first = Chunk(0, 0)
            x_hi(first)
            split_hi(("s",))
            copy_lgT(first)

            def chunk(ch, c):
                late = 1 if c == 0 else 0
                for k in range(SLOTS):
                    if c == 0 and k == 1:
                        router_silus(ch)
                        split_hi(("g", "u", "o"))
                        copy_cwT(ch, False)
                    if k == late and has(c, 1):
                        x_hi(ch.at(1))
                    if c == 0 and k == 2:
                        split_hi(("sd", "d"))
                    if k == 2 + late and has(c, 1):
                        copy_lgT(ch.at(1))
                    if k == 3 and has(c, -1):
                        ffn_silu(ch.at(-1))
                    if k == 5 and has(c, 1):
                        router_silus(ch.at(1))
                    if k < NH:
                        rec_in(ch, k)
                    else:
                        silu(ch, k, c)
                    if k == 0 and has(c, -1):
                        ffn_hi(ch.at(-1), SLOTS - 1)
                    if k in (2, 3):
                        rec_hi(ch, k - 2)
                    if k == 10 and has(c, 1):
                        copy_cwT(ch.at(1), True)
                    if k > NH:
                        ffn_hi(ch, k - 1)

            chunks(act, chunk)
            last = Chunk(NCH // 2 - 1, 1)
            ffn_hi(last, SLOTS - 1)
            ffn_silu(last)

        @block.vector
        def _(dve):
            def ln_stats(ch):
                dve.wait_ge(s_xin[ch.par], ch.dma())
                for t in range(TT):
                    last = nc.vector.bn_stats(stats[:, t], x_in[:, ch.par, t])
                last.then_inc(s_stat, 1)

            def ln_stats_landed(ch):
                dve.wait_ge(s_stat, ch.n(1, 1))

            def ln_mean_var(ch):
                for t in range(TT):
                    last = nc.vector.bn_aggr(meanvar[:, t], stats[:, t])
                last.then_inc(s_mv, 1)

            def normalise(ch, tiles, reused):
                dve.wait_ge(s_rstd, ch.n(1, 1))
                if reused:
                    dve.wait_ge(s_xT, ch.at(-1).n(1, 1))
                for t in tiles:
                    last = nc.vector.tensor_scalar(xn[:, t], x_in[:, ch.par, t], meanvar[:, t, 0:1], rstd[:, t:t + 1],
                                                   ALU.subtract, ALU.mult)
                if TT - 1 in tiles:
                    last.then_inc(s_norm, 1)

            def x_lo(ch):
                dve.wait_ge(s_xhi, ch.n(1, 1))
                nc.vector.tensor_tensor(xT_lo[:, ch.par], p_front[:, :], xT_hi[:, ch.par].bitcast(F32), ALU.subtract)\
                  .then_inc(s_xlo, 1)

            def split_lo(names):
                for n, (name, cols) in enumerate(WCOLS):
                    if name in names:
                        w = slice(off[name], off[name] + cols)
                        dve.wait_ge(s_hi_w, n + 1)
                        nc.vector.tensor_tensor(w_lo[:, w], stage[:, w], w_hi[:, w].bitcast(F32), ALU.subtract)\
                          .then_inc(s_lo_w, 1)

            def rec_scan(ch, j):
                dve.wait_ge(s_a, ch.n(NH, j + 1))
                dve.wait_ge(s_relu, ch.n(NH, j + 1))
                nc.vector.scalar_tensor_tensor(out=rec_v[:, j], in0=rec_v[:, j], scalar=0.5, in1=rec_z[:, j],
                                               op0=ALU.add, op1=ALU.mult).then_inc(s_v, 1)
                dve.wait_ge(s_v, ch.n(NH, j + 1))
                for q in range(SEQS):
                    w = slice(q * S, (q + 1) * S)
                    last = nc.vector.tensor_tensor_scan(rec_h[:, j, w], rec_a[:, j, w], rec_v[:, j, w], 0.0,
                                                        ALU.mult, ALU.add)
                last.then_inc(s_scan, 1)

            def gated(ch, k):
                f, par = k - NH, slot_par(ch, k)
                dve.wait_ge(s_silu, ch.n(NF, f + 1))
                dve.wait_ge(s_lin, ch.n(SLOTS, k + 1))
                nc.vector.tensor_tensor(prod[:, f], p_lin[par][:, :], silu_g[:, par], ALU.mult).then_inc(s_p, 1)

            def weighted(ch, k):
                f = k - NH
                if f == 1:
                    dve.wait_ge(s_cwa[ch.par], ch.dma(2))
                if f == 1 + NB // 2:
                    dve.wait_ge(s_cwb[ch.par], ch.dma(2))
                dve.wait_ge(s_p, ch.n(NF, f + 1))
                nc.vector.tensor_tensor(prod[:, f], prod[:, f], cw[:, ch.par, f - 1], ALU.mult).then_inc(s_q, 1)

            def router_sum(ch):
                dve.wait_ge(s_lt, ch.n(1, 1))
                both = p_front[:, 0:TT * 2 * E].rearrange("p (t h e) -> p t e h", t=TT, h=2)
                nc.vector.tensor_reduce(lg[:, :, :], both, AX.X, ALU.add).then_inc(s_rt, 1)

            def router_sum_landed(ch):
                dve.wait_ge(s_rt, ch.n(ROUTER_STEPS, 1))

            def router_max(ch):
                for t in range(TT):
                    last = nc.vector.max(top8[:, t], lg[:, t])
                last.then_inc(s_rt, 1)

            def router_index(ch):
                dve.wait_ge(s_rt, ch.n(ROUTER_STEPS, 2))
                nc.vector.tensor_tensor(shifted[:, :, :], lg[:, :, :], top8[:, :, 0:1].to_broadcast([P, TT, E]),
                                        ALU.subtract).then_inc(s_shift, 1)
                for t in range(TT):
                    last = nc.vector.max_index(top8_at[:, t], top8[:, t], lg[:, t])
                last.then_inc(s_rt, 1)

            def router_inverse(ch):
                dve.wait_ge(s_rsil, ch.n(1, 1))
                nc.vector.reciprocal(expv[:, :, :], silu_p[:, :, :]).then_inc(s_rt, 1)

            def router_exp(ch):
                dve.wait_ge(s_rt, ch.n(ROUTER_STEPS, 6))
                nc.vector.scalar_tensor_tensor(out=expv[:, :, :], in0=silu_n[:, :, :], scalar=-1.0,
                                               in1=expv[:, :, :], op0=ALU.mult, op1=ALU.mult).then_inc(s_rt, 1)

            def router_total(ch):
                dve.wait_ge(s_rt, ch.n(ROUTER_STEPS, 7))
                nc.vector.tensor_reduce(esum[:, :], expv[:, :, :], AX.X, ALU.add).then_inc(s_rt, 1)

            def router_mask(ch):
                at0, at1 = (top8_at[:, :, n:n + 1].to_broadcast([P, TT, E]) for n in range(2))
                experts = iota_e[:, :].rearrange("p (t e) -> p t e", t=1).to_broadcast([P, TT, E])
                dve.wait_ge(s_rt, ch.n(ROUTER_STEPS, 3))
                nc.vector.tensor_tensor(mask0[:, :, :], experts, at0, ALU.is_equal)
                nc.vector.tensor_tensor(mask1[:, :, :], experts, at1, ALU.is_equal).then_inc(s_rt, 1)

            def router_masks_joined(ch):
                dve.wait_ge(s_rt, ch.n(ROUTER_STEPS, 4))
                nc.vector.tensor_tensor(mask0[:, :, :], mask0[:, :, :], mask1[:, :, :], ALU.add).then_inc(s_rt, 1)

            def router_select(ch):
                dve.wait_ge(s_rt, ch.n(ROUTER_STEPS, 8))
                nc.vector.tensor_tensor(mask0[:, :, :], mask0[:, :, :], expv[:, :, :], ALU.mult)
                nc.vector.reciprocal(rsum[:, :], esum[:, :]).then_inc(s_rt, 1)

            def router_weights(ch):
                dve.wait_ge(s_rt, ch.n(ROUTER_STEPS, 9))
                nc.vector.tensor_tensor(cw_tok[:, 0:E, :].rearrange("p e t -> p t e"), mask0[:, :, :],
                                        rsum[:, :].rearrange("p (t e) -> p t e", e=1).to_broadcast([P, TT, E]),
                                        ALU.mult).then_inc(s_cwtok, 1)

            def gate_out(ch):
                dve.wait_ge(s_gsil, ch.n(1, 1))
                dve.wait_ge(s_rec, ch.n(1, 1))
                nc.vector.tensor_tensor(sg[:, :], p_rec[:, :], ffn_gate[:, :], ALU.mult).then_inc(s_sg, 1)

            def add_out(ch):
                dve.wait_ge(s_ot, ch.n(1, 1))
                dve.wait_ge(s_xres[ch.par], ch.dma())
                res = x_out[:, ch.par].rearrange("p t d -> p (t d)")
                nc.vector.tensor_tensor(res, p_out[:, :], res, ALU.add).then_inc(s_add, 1)

            first, second = Chunk(0, 0), Chunk(0, 1)
            ln_stats(first)
            ln_stats_landed(first)
            ln_mean_var(first)
            dve.wait_ge(s_const, CONSTS)
            normalise(first, range(TT), False)
            split_lo(("r",))
            dve.wait_ge(s_lo_w, 1)
            nc.vector.tensor_copy(wr_both[:, 0:E], w_hi[:, 0:E].bitcast(F32))
            nc.vector.tensor_copy(wr_both[:, E:2 * E], w_lo[:, 0:E].bitcast(F32)).then_inc(s_lo_w, 1)
            split_lo(("hg",))
            x_lo(first)
            ln_stats(second)
            ln_stats_landed(second)
            ln_mean_var(second)
            split_lo(("s",))
            normalise(second, range(TT), True)
            router_sum(first)
            router_sum_landed(first)
            router_max(first)
            router_index(first)
            for link in (router_mask, router_masks_joined, router_inverse, router_exp, router_total, router_select,
                         router_weights):
                link(first)
            split_lo(("g",))

            def chunk(ch, c):
                ahead, ahead2, behind = has(c, 1), has(c, 2), has(c, -1)
                late = 1 if c == 0 else 0
                for k in range(SLOTS):
                    if k == late and ahead:
                        x_lo(ch.at(1))
                    if k in (1, 2):
                        rec_scan(ch, k - 1)
                    if c == 0 and k == 1:
                        split_lo(("u", "o"))
                    if c == 0 and k == 2:
                        split_lo(("sd", "d"))
                    if k == 3 and behind:
                        gate_out(ch.at(-1))
                    if k == 5 and behind:
                        add_out(ch.at(-1))
                    if k == 5 and ahead2:
                        ln_stats_landed(ch.at(2))
                    if k >= NH:
                        gated(ch, k)
                    if k == 3 and ahead:
                        router_sum(ch.at(1))
                        router_sum_landed(ch.at(1))
                    if k == 5 and ahead:
                        router_mask(ch.at(1))
                    if k == 6 and ahead:
                        router_inverse(ch.at(1))
                    if k == 7 and ahead:
                        router_total(ch.at(1))
                    if k == 8 and ahead:
                        router_weights(ch.at(1))
                    if k == 4 and ahead2:
                        ln_stats(ch.at(2))
                    if k == 5 and ahead2:
                        ln_mean_var(ch.at(2))
                    if k == 8 and ahead2:
                        normalise(ch.at(2), range(TT // 2), True)
                    if k == 9 and ahead2:
                        normalise(ch.at(2), range(TT // 2, TT), True)
                    if k > NH:
                        weighted(ch, k)
                    if k == 3 and ahead:
                        router_max(ch.at(1))
                    if k == 4 and ahead:
                        router_index(ch.at(1))
                    if k == 6 and ahead:
                        router_exp(ch.at(1))
                    if k == 5 and ahead:
                        router_masks_joined(ch.at(1))
                    if k == 7 and ahead:
                        router_select(ch.at(1))

            chunks(dve, chunk)
            last = Chunk(NCH // 2 - 1, 1)
            gate_out(last)
            add_out(last)

        @block.tensor
        def _(pe):
            split_count = {}
            for n, (name, _) in enumerate(WCOLS):
                split_count[name] = n + 1 + (n > 0)

            def split_product(acc, name, col, hi, lo, start, stop):
                w = slice(off[name] + col * P, off[name] + (col + 1) * P)
                nc.tensor.matmul(acc, w_hi[:, w], hi, start=start, stop=False)
                nc.tensor.matmul(acc, w_hi[:, w], lo, start=False, stop=False)
                return nc.tensor.matmul(acc, w_lo[:, w], hi, start=False, stop=stop)

            def transpose_x(ch, reused):
                pe.wait_ge(s_norm, ch.n(1, 1))
                if reused:
                    pe.wait_ge(s_rt, ch.at(-1).n(ROUTER_STEPS, 1))
                for t in range(TT):
                    last = nc.tensor.transpose(p_front[:, t * P:(t + 1) * P], xn[:, t], ident[:, :])
                last.then_inc(s_xT, 1)

            def router_logits(ch):
                pe.wait_ge(s_xlo, ch.n(1, 1))
                nc.tensor.matmul(p_front[0:2 * E, :], wr_both[:, :], xT_hi[:, ch.par], start=True, stop=False)
                nc.tensor.matmul(p_front[0:2 * E, :], wr_both[:, :], xT_lo[:, ch.par], start=False, stop=True)\
                  .then_inc(s_rl, 1)

            def transpose_logits(ch):
                pe.wait_ge(s_const, CONSTS)
                pe.wait_ge(s_lgT, ch.n(1, 1))
                for t in range(TT):
                    last = nc.tensor.transpose(p_front[:, t * 2 * E:(t + 1) * 2 * E], lgT[:, t * P:(t + 1) * P],
                                               ident[0:2 * E, 0:2 * E])
                last.then_inc(s_lt, 1)

            def transpose_cw(ch, reused):
                if reused:
                    pe.wait_ge(s_add, ch.at(-2).n(1, 1))
                pe.wait_ge(s_cwtok, ch.n(1, 1))
                nc.tensor.transpose(p_out[:, 0:P], cw_tok[:, :, :].rearrange("p e t -> p (e t)"),
                                    ident[:, :]).then_inc(s_cwTp, 1)

            def up(ch, k, c):
                par = slot_par(ch, k)
                hi, lo = xT_hi[:, ch.par], xT_lo[:, ch.par]
                former, fk = (ch, k - 2) if k >= 2 else (ch.at(-1), k - 2 + SLOTS)
                known = k >= 2 or has(c, -1)
                if k < NH:
                    gate, lin = ("hg", NH + k), ("hg", k)
                elif k == NH:
                    gate, lin = ("s", 0), ("s", 1)
                else:
                    gate, lin = ("g", k - NH - 1), ("u", k - NH - 1)
                if c == 0:
                    pe.wait_ge(s_lo_w, split_count[lin[0]])
                if known and fk < NH:
                    pe.wait_ge(s_tanh, former.n(NH, fk + 1))
                elif known:
                    pe.wait_ge(s_silu, former.n(NF, fk - NH + 1))
                split_product(p_gate[par][:, :], *gate, hi, lo, True, True).then_inc(s_gate, 1)
                if known and fk < NH:
                    pe.wait_ge(s_relu, former.n(NH, fk + 1))
                elif known:
                    pe.wait_ge(s_p, former.n(NF, fk - NH + 1))
                split_product(p_lin[par][:, :], *lin, hi, lo, True, True).then_inc(s_lin, 1)

            def down(ch, k, c):
                f = k - NH
                if f == 0 and c == 0:
                    pe.wait_ge(s_lo_w, split_count["d"])
                if f == 0 and has(c, -1):
                    pe.wait_ge(s_gsil, ch.at(-1).n(1, 1))
                pe.wait_ge(s_flo, ch.n(NF, f + 1))
                split_product(p_ffn[:, :], "sd" if f == 0 else "d", max(f - 1, 0), act_hi[:, k], act_lo[:, k],
                              f == 0, f == NF - 1).then_inc(s_down, 1)

            def rec_down(ch, j, c):
                if j == 0 and has(c, -1):
                    pe.wait_ge(s_sg, ch.at(-1).n(1, 1))
                pe.wait_ge(s_hlo, ch.n(NH, j + 1))
                last = split_product(p_rec[:, :], "o", j, act_hi[:, j], act_lo[:, j], j == 0, j == NH - 1)
                if j == NH - 1:
                    last.then_inc(s_rec, 1)

            def transpose_out(ch, reused):
                pe.wait_ge(s_sg, ch.n(1, 1))
                if reused:
                    pe.wait_ge(s_cwT, ch.at(1).n(1, 1))
                for t in range(TT):
                    last = nc.tensor.transpose(p_out[:, t * P:(t + 1) * P], sg[:, t * P:(t + 1) * P], ident[:, :])
                last.then_inc(s_ot, 1)

            first = Chunk(0, 0)
            pe.wait_ge(s_const, CONSTS)
            transpose_x(first, False)
            pe.wait_ge(s_lo_w, 2)
            router_logits(first)

            def chunk(ch, c):
                ahead, behind = has(c, 1), has(c, -1)
                late = 1 if c == 0 else 0
                for k in range(SLOTS):
                    if k == late and ahead:
                        transpose_x(ch.at(1), True)
                    up(ch, k, c)
                    if c == 0 and k == 0:
                        transpose_logits(ch)
                    if c == 0 and k == 1:
                        transpose_cw(ch, False)
                    if k == 1 + late and ahead:
                        router_logits(ch.at(1))
                    if k == 2 + late and ahead:
                        transpose_logits(ch.at(1))
                    if k < LAG and behind:
                        down(ch.at(-1), k - LAG + SLOTS, None)
                    if k == 4 and behind:
                        transpose_out(ch.at(-1), True)
                    if k in (4, 5):
                        rec_down(ch, k - 4, c)
                    if k == 10 and ahead:
                        transpose_cw(ch.at(1), behind)
                    if k - LAG >= NH:
                        down(ch, k - LAG, c)

            chunks(pe, chunk)
            last = Chunk(NCH // 2 - 1, 1)
            for k in range(SLOTS - LAG, SLOTS):
                down(last, k, None)
            transpose_out(last, False)


_INS = ["L0_attn_x", "L0_attn_W_hg", "L0_attn_W_out", "L0_ffn_Wr", "L0_ffn_Wg", "L0_ffn_Wu", "L0_ffn_Wd",
        "L0_ffn_Sg", "L0_ffn_Su", "L0_ffn_Sd"]


def kernel(**inputs):
    import numpy as _np
    import concourse.bacc as _bacc
    from concourse import mybir as _mybir
    from concourse.bass_utils import run_bass_kernel_spmd as _run

    nc = _bacc.Bacc("TRN2", target_bir_lowering=False, num_devices=1)
    arrays, args = {}, []
    for name in _INS:
        a = _np.ascontiguousarray(inputs[name])
        arrays[f"in_{name}"] = a
        args.append(nc.dram_tensor(f"in_{name}", a.shape, _mybir.dt.from_np(a.dtype), kind="ExternalInput").ap())
    shape = arrays["in_L0_attn_x"].shape
    result = nc.dram_tensor("out_x", shape, _mybir.dt.float32, kind="ExternalOutput").ap()
    recurrent_moe_block(nc, *args, result)
    r = _run(nc, [arrays], core_ids=[0])
    return r.results[0]["out_x"]
```
